# Optimizing a Trainium2 kernel written in Bass

```python
import numpy as np
import jax
import jax.numpy as jnp

def _softmax(x, axis=-1):
    return jax.nn.softmax(x, axis=axis)

def _gelu(x):
    return jax.nn.gelu(x, approximate=True)

def _silu(x):
    return jax.nn.silu(x)

def _sigmoid(x):
    return jax.nn.sigmoid(x)

def _layernorm(x, axis=-1, eps=1e-05):
    m = jnp.mean(x, axis=axis, keepdims=True)
    v = jnp.var(x, axis=axis, keepdims=True)
    return (x - m) / jnp.sqrt(v + eps)

def _scatter_add(tgt, idx, src, axis=0):
    return tgt.at[idx].add(src)

def _segment_sum(src, seg, n):
    return jax.ops.segment_sum(src, seg, n)
kernel_name = 'mk_cond_resid_d4_seqx_r8_f49250'

def setup_inputs(seed: int=0):
    np.random.seed(seed)
    _w = jnp.asarray

    def _rec_inputs():
        import jax
        import jax.numpy as jnp
        _rk = jax.random.key(seed)
        x = -0.000125 + 0.9999 * jax.random.normal(jax.random.fold_in(_rk, 1), (8, 128, 512), jnp.float32)
        _lenS = 128 - jax.random.randint(jax.random.fold_in(_rk, 7), (8,), 0, max(1, 128 // 4) + 1, jnp.int32)
        _lenS2 = 128 - jax.random.randint(jax.random.fold_in(_rk, 8), (8,), 0, max(1, 128 // 4) + 1, jnp.int32)
        itok_B_3_7 = jax.random.randint(jax.random.fold_in(_rk, 11), (8,), 3, 8, jnp.int32)
        itok_B_0_15 = jax.random.randint(jax.random.fold_in(_rk, 12), (8,), 0, 16, jnp.int32)
        itok_B_0_7 = jax.random.randint(jax.random.fold_in(_rk, 13), (8,), 0, 8, jnp.int32)
        return (x, itok_B_3_7, itok_B_0_15, itok_B_0_7)
    x, itok_B_3_7, itok_B_0_15, itok_B_0_7 = _rec_inputs()

    def _L0_cond_setup():
        import jax, jax.numpy as jnp
        import numpy as np
        RANK = 16
        ALPHA = 16.0
        SCALING = ALPHA / RANK
        N_ADAPTERS = 8
        IN_F = 512
        OUT_F = 512
        BATCH = 4
        SEQ = 256
        key = jax.random.key(seed)
        kx, ka, kb, ki = jax.random.split(key, 4)
        x = jax.random.normal(kx, (BATCH, SEQ, IN_F), dtype=jnp.float32)
        A = jax.random.normal(ka, (N_ADAPTERS, OUT_F, RANK), dtype=jnp.float32) * 0.02
        B = jax.random.normal(kb, (N_ADAPTERS, RANK, IN_F), dtype=jnp.float32) * 0.02
        adapter_ids = jax.random.randint(ki, (BATCH,), 0, N_ADAPTERS, dtype=jnp.int32)
        return {'x': x, 'A': A, 'B': B, 'adapter_ids': adapter_ids}
    _L0_cond_all = _L0_cond_setup()
    _L0_cond_in = {k: v for k, v in _L0_cond_all.items() if k in ('A', 'B')}
    del _L0_cond_all

    def _L1_cond_setup():
        import jax, jax.numpy as jnp
        import numpy as np
        SCALING = 16.0 / 16
        key = jax.random.key(seed)
        k1, k2, k3, k4, k5 = jax.random.split(key, 5)
        B, S, D_IN, D_OUT, R, N_ADPT = (8, 256, 512, 512, 16, 16)
        x = jax.random.normal(k1, (B, S, D_IN), dtype=jnp.float32)
        adapter_indices = jax.random.randint(k2, (B,), 0, N_ADPT, dtype=jnp.int32)
        W = jax.random.normal(k3, (D_IN, D_OUT), dtype=jnp.float32) * 0.02
        lora_A = jax.random.normal(k4, (N_ADPT, D_IN, R), dtype=jnp.float32) * 0.02
        lora_B = jax.random.normal(k5, (N_ADPT, R, D_OUT), dtype=jnp.float32) * 0.02
        return {'x': x, 'adapter_indices': adapter_indices, 'W': W, 'lora_A': lora_A, 'lora_B': lora_B}
    _L1_cond_all = _L1_cond_setup()
    _L1_cond_in = {k: v for k, v in _L1_cond_all.items() if k in ('W', 'lora_A', 'lora_B')}
    del _L1_cond_all

    def _L2_cond_setup():
        import jax, jax.numpy as jnp
        import numpy as np
        MAX_LORAS, OUT, IN = (8, 512, 512)
        B, S = (4, 256)
        key = jax.random.key(seed)
        k1, k2, k3 = jax.random.split(key, 3)
        x = jax.random.normal(k1, (B, S, IN), dtype=jnp.float32)
        weight = jax.random.normal(k2, (MAX_LORAS, OUT, IN), dtype=jnp.float32) * 0.02
        adapter_ids = jax.random.randint(k3, (B,), 0, MAX_LORAS, dtype=jnp.int32)
        return {'x': x, 'weight': weight, 'adapter_ids': adapter_ids}
    _L2_cond_all = _L2_cond_setup()
    _L2_cond_in = {k: v for k, v in _L2_cond_all.items() if k in ('weight',)}
    del _L2_cond_all

    def _L3_cond_setup():
        import jax, jax.numpy as jnp
        import numpy as np
        TOP_K = 2
        LANG_BIAS = 5.0
        SCALING = 32.0 / 16.0
        LANGUAGE_PAD_ID = -1
        key = jax.random.key(seed)
        ks = jax.random.split(key, 6)
        B, T, D, O, E, R = (4, 256, 512, 512, 8, 16)
        x = jax.random.normal(ks[0], (B, T, D), dtype=jnp.float32)
        language_ids = jax.random.randint(ks[1], (B,), 0, E).astype(jnp.int64)
        W = jax.random.normal(ks[2], (O, D), dtype=jnp.float32) * (1.0 / np.sqrt(D))
        Wr = jax.random.normal(ks[3], (E, D), dtype=jnp.float32) * (1.0 / np.sqrt(D))
        A = jax.random.normal(ks[4], (E, R, D), dtype=jnp.float32) * (1.0 / np.sqrt(D))
        Bm = jax.random.normal(ks[5], (O, R), dtype=jnp.float32) * 0.0
        Bm = jnp.broadcast_to(Bm, (E, O, R)) + jax.random.normal(ks[5], (E, O, R), dtype=jnp.float32) * 0.02
        return {'x': x, 'language_ids': language_ids, 'W': W, 'Wr': Wr, 'A': A, 'B': Bm}
    _L3_cond_all = _L3_cond_setup()
    _L3_cond_in = {k: v for k, v in _L3_cond_all.items() if k in ('W', 'Wr', 'A', 'B')}
    del _L3_cond_all
    return {'x': x, 'itok_B_3_7': itok_B_3_7, 'itok_B_0_15': itok_B_0_15, 'itok_B_0_7': itok_B_0_7, 'L0_cond_A': _L0_cond_in['A'], 'L0_cond_B': _L0_cond_in['B'], 'L1_cond_W': _L1_cond_in['W'], 'L1_cond_lora_A': _L1_cond_in['lora_A'], 'L1_cond_lora_B': _L1_cond_in['lora_B'], 'L2_cond_weight': _L2_cond_in['weight'], 'L3_cond_W': _L3_cond_in['W'], 'L3_cond_Wr': _L3_cond_in['Wr'], 'L3_cond_A': _L3_cond_in['A'], 'L3_cond_B': _L3_cond_in['B']}

def reference(x, itok_B_3_7, itok_B_0_15, itok_B_0_7, L0_cond_A, L0_cond_B, L1_cond_W, L1_cond_lora_A, L1_cond_lora_B, L2_cond_weight, L3_cond_W, L3_cond_Wr, L3_cond_A, L3_cond_B):
    import jax
    import jax.numpy as jnp

    def _L0_cond_ref(x, A, B, adapter_ids):
        import jax, jax.numpy as jnp
        import numpy as np
        RANK = 16
        ALPHA = 16.0
        SCALING = ALPHA / RANK
        N_ADAPTERS = 8
        IN_F = 512
        OUT_F = 512
        BATCH = 4
        SEQ = 256
        B_sel = B[adapter_ids]
        A_sel = A[adapter_ids]
        Bx = jnp.einsum('bni,bri->bnr', x, B_sel)
        out = jnp.einsum('bnr,bor->bno', Bx, A_sel)
        return out * SCALING

    def _L1_cond_ref(x, adapter_indices, W, lora_A, lora_B):
        import jax, jax.numpy as jnp
        import numpy as np
        SCALING = 16.0 / 16
        base_out = jnp.einsum('bsi,io->bso', x, W)
        A = lora_A[adapter_indices]
        Bm = lora_B[adapter_indices]
        xr = jnp.einsum('bsi,bir->bsr', x, A)
        lora_out = jnp.einsum('bsr,bro->bso', xr, Bm)
        return base_out + lora_out * SCALING

    def _L2_cond_ref(x, weight, adapter_ids):
        import jax, jax.numpy as jnp
        import numpy as np
        MAX_LORAS, OUT, IN = (8, 512, 512)
        B, S = (4, 256)
        w = weight[adapter_ids]
        return jnp.einsum('bsi,boi->bso', x, w)

    def _L3_cond_ref(x, language_ids, W, Wr, A, B):
        import jax, jax.numpy as jnp
        import numpy as np
        TOP_K = 2
        LANG_BIAS = 5.0
        SCALING = 32.0 / 16.0
        LANGUAGE_PAD_ID = -1
        base = jnp.einsum('btd,od->bto', x, W)
        E = Wr.shape[0]
        logits = jnp.einsum('btd,ed->bte', x.astype(jnp.float32), Wr.astype(jnp.float32))
        expert_targets = language_ids
        valid = expert_targets >= 0
        tgt = jnp.where(valid, expert_targets, 0)
        bias = jax.nn.one_hot(tgt, E, dtype=logits.dtype) * LANG_BIAS
        bias = jnp.where(valid[:, None], bias, 0.0)
        logits = logits + bias[:, None, :]
        topw, topi = jax.lax.top_k(logits, TOP_K)
        weights = jax.nn.softmax(topw, axis=-1)
        gates = jnp.sum(jax.nn.one_hot(topi, E, dtype=weights.dtype) * weights[..., None], axis=-2)
        gates = gates.astype(x.dtype)
        h = jnp.einsum('btd,erd->bter', x, A)
        lora_out = jnp.einsum('bter,bte,eor->bto', h, gates, B)
        return base + SCALING * lora_out
    x = x + _L0_cond_ref(x, L0_cond_A, L0_cond_B, itok_B_3_7)
    x = x + _L1_cond_ref(x, itok_B_0_15, L1_cond_W, L1_cond_lora_A, L1_cond_lora_B)
    x = x + _L2_cond_ref(x, L2_cond_weight, itok_B_3_7)
    x = x + _L3_cond_ref(x, itok_B_0_7, L3_cond_W, L3_cond_Wr, L3_cond_A, L3_cond_B)
    return x

_drawn_inputs = setup_inputs


def setup_inputs(seed=0):
    import zlib

    import numpy as np

    out = dict(_drawn_inputs(seed))
    spreads = {}
    factors = {'L3_cond_Wr': 3.977}
    for name, (base, spread) in spreads.items():
        noise = np.random.default_rng([zlib.crc32(name.encode()), seed]).standard_normal(out[name].shape)
        drawn = base * np.exp(spread * noise) if base else spread * noise
        out[name] = jnp.asarray(drawn.astype(out[name].dtype))
    for name, factor in factors.items():
        out[name] = (out[name] * factor).astype(out[name].dtype)
    return out
```

```python
from contextlib import ExitStack

import concourse.bass as bass
from concourse import mybir

F32 = mybir.dt.float32
F32R = mybir.dt.float32r
BF16 = mybir.dt.bfloat16
I32 = mybir.dt.int32
U32 = mybir.dt.uint32
ALU = mybir.AluOpType
ACT = mybir.ActivationFunctionType

P = 128
D = 512
K = D // P
B = 8
HB = B // 2
T = HB * P
R = 16
E = 8
HR = HB * R
AR = E * R + E
LANG_BIAS = 5.0
WARM_UP = 16
STAGES = 4

C_GMASK = 0
C_UVMASK = C_GMASK + P
C_IOTA = C_UVMASK + HB
C_COLS = C_IOTA + E
I_ROW0, I_ROW1, I_RANK, I_LANG, I_W2 = 0, 1, 2, 3, 3 + B
I_COLS = 3 + 2 * B

LOADS = ["x0", "w1", "w2_0", "w3", "w2_1", "w2_2", "w2_3", "x1", "w2_4", "w2_5", "w2_6", "w2_7"]
SLOT = {name: i % STAGES for i, name in enumerate(LOADS)}


def cond_resid_kernel(nc, consts, ints, xT, w1, gather0, gather1, w2T, w3T, ar, b3, out):
    with ExitStack() as ctx:
        def sb(name, shape, dt=F32):
            return ctx.enter_context(nc.sbuf_tensor(name, shape, dt))

        def sem(name):
            return ctx.enter_context(nc.semaphore(name))

        cst = sb("cst", [P, C_COLS])
        eye = sb("eye", [P, P])
        ids = sb("ids", [P, I_COLS], I32)
        rows = sb("rows", [P, 2], U32)
        stage = sb("stage", [P, STAGES, K, D])
        x_hi, x_lo = sb("x_hi", [P, K, T], F32R), sb("x_lo", [P, K, T], F32R)
        w1_hi, w1_lo = sb("w1_hi", [P, K, D], F32R), sb("w1_lo", [P, K, D], F32R)
        w2_hi, w2_lo = sb("w2_hi", [P, 2, K, D], F32R), sb("w2_lo", [P, 2, K, D], F32R)
        w3_hi, w3_lo = sb("w3_hi", [P, K, D], F32R), sb("w3_lo", [P, K, D], F32R)
        ar_in = sb("ar_in", [P, K, AR])
        ar_hi, ar_lo = sb("ar_hi", [P, K, AR], F32R), sb("ar_lo", [P, K, AR], F32R)
        b3_in = sb("b3_in", [P, D])
        b3_hi, b3_lo = sb("b3_hi", [P, D], F32R), sb("b3_lo", [P, D], F32R)
        g0 = sb("g0", [P, 2, D])
        g1 = sb("g1", [P, 2, D])
        a0_hi, a0_lo = sb("a0_hi", [P, K, P], F32R), sb("a0_lo", [P, K, P], F32R)
        a1 = sb("a1", [P, K, P])
        a1_hi, a1_lo = sb("a1_hi", [P, K, P], F32R), sb("a1_lo", [P, K, P], F32R)
        b0_hi, b0_lo = sb("b0_hi", [P, D], F32R), sb("b0_lo", [P, D], F32R)
        gm = sb("gm", [P, P])
        g_hi, g_lo = sb("g_hi", [P, P], F32R), sb("g_lo", [P, P], F32R)
        dn_hi, dn_lo = sb("dn_hi", [P, K, 2, P], F32R), sb("dn_lo", [P, K, 2, P], F32R)
        up_hi, up_lo = sb("up_hi", [P, 2, D], F32R), sb("up_lo", [P, 2, D], F32R)
        uv = sb("uv", [P, T])
        uv_hi, uv_lo = sb("uv_hi", [P, T], F32R), sb("uv_lo", [P, T], F32R)
        x2_hi, x2_lo = sb("x2_hi", [P, K, T], F32R), sb("x2_lo", [P, K, T], F32R)
        x3 = sb("x3", [P, 2, D])
        x3_hi, x3_lo = sb("x3_hi", [P, 2, K, P], F32R), sb("x3_lo", [P, 2, K, P], F32R)
        onehot = sb("onehot", [P, B, E])
        bias = sb("bias", [P, B, E], F32R)
        ones = sb("ones", [P, P], F32R)
        top = sb("top", [P, 2, 8])
        topi = sb("topi", [P, 2, 8], U32)
        hot = sb("hot", [P, 2, 2, E])
        gap = sb("gap", [P, 2, 1])
        ex = sb("ex", [P, 2, 1])
        rden = sb("rden", [P, 2, 2])
        gate = sb("gate", [P, 2, E])
        hg = sb("hg", [P, 2, P])
        hg_hi, hg_lo = sb("hg_hi", [P, 2, P], F32R), sb("hg_lo", [P, 2, P], F32R)
        res = sb("res", [P, 2, D])
        warm = x3[:, 0, 0:D // 2].bitcast(BF16)

        bank = [ctx.enter_context(nc.psum_tensor(f"bank{i}", [P, D], F32)) for i in range(8)]
        L1_BANK, X3_BANK, X3T_BANK, AR_BANK, OUT_BANK, HGT_BANK, UV_BANK = 0, 0, 2, 3, 4, 6, 7
        A0T_BANK, A1T_BANK, B0T_BANK, G_BANK, BG_BANK, AW_BANK = 4, 5, 6, 7, 6, 4

        cst_in, ids_in = sem("cst_in"), sem("ids_in")
        x_in = [sem(f"x_in{k}") for k in range(K)]
        w1_in = [sem(f"w1_in{k}") for k in range(K)]
        w2_in = [sem(f"w2_in{i}") for i in range(4)]
        w3_in, ar_dma, b3_dma = sem("w3_in"), sem("ar_dma"), sem("b3_dma")
        g0_in, g1_in = sem("g0_in"), sem("g1_in")
        out_done = [sem(f"out_done{i}") for i in range(2)]
        w1_eye, w2_eye, w3_eye, rows_ok = sem("w1_eye"), sem("w2_eye"), sem("w3_eye"), sem("rows_ok")
        eye_zero, eye_ok = sem("eye_zero"), sem("eye_ok")
        S = {}
        for n in ("x", "w1", "w2", "w3", "ar", "b3", "a0", "a1", "b0", "g", "dnu", "dnv", "up", "uv", "x2",
                  "x3t", "hgt"):
            S[n + "_hi"], S[n + "_lo"] = sem(n + "_hi_ok"), sem(n + "_lo_ok")
        a1_ok, gm_ok, a1g_ok, up_ok = (sem(n) for n in ("a1_ok", "gm_ok", "a1g_ok", "up_ok"))
        uv_ok, x3_ok, res_ok = (sem(n) for n in ("uv_ok", "x3_ok", "res_ok"))
        bias_ok, gap_ok, ex_ok, hg_ok, chain = (sem(n) for n in ("bias_ok", "gap_ok", "ex_ok", "hg_ok", "chain"))
        warm_ok = sem("warm_ok")
        a0t_mm, a1t_mm, b0t_mm, g_mm, bg_mm, aw_mm = (sem(n) for n in
                                                      ("a0t_mm", "a1t_mm", "b0t_mm", "g_mm", "bg_mm", "aw_mm"))
        uv_mm, l1x_mm, x2_mm, x3_mm, x3t_mm = (sem(n) for n in ("uv_mm", "l1x_mm", "x2_mm", "x3_mm", "x3t_mm"))
        ar_mm, hgt_mm, out_mm = (sem(n) for n in ("ar_mm", "hgt_mm", "out_mm"))

        iota = cst[:, C_IOTA:C_IOTA + E]

        def slot(name):
            return stage[:, SLOT[name]]

        def diagonal(w):
            return bass.AP(w.tensor, w.offset, [list(w.ap[0]), [D + P, K], [1, P]])

        ident = eye[:]

        block = ctx.enter_context(nc.Block())

        @block.sync
        def _(sp):
            sp.dma_start(ids[:], ints).then_inc(ids_in, 16)
            for k in range(K):
                sp.dma_start(slot("w1")[:, k], w1[k]).then_inc(w1_in[k], 16)
                sp.dma_start(slot("x0")[:, k], xT[0, k]).then_inc(x_in[k], 16)
                if k == 1:
                    sp.dma_start(cst[:], consts).then_inc(cst_in, 16)
            sp.wait_ge(ids_in, 16)

            def load_w2(b):
                adapter = sp.value_load(ids[0:1, I_W2 + b:I_W2 + b + 1], min_val=0, max_val=E - 1)
                sp.dma_start(slot(f"w2_{b}"), w2T[bass.DynSlice(adapter, 1)].rearrange("e p k o -> p (e k) o")) \
                    .then_inc(w2_in[b % 4], 16)

            sp.wait_ge(g0_in, 16)
            sp.dma_start(ar_in[:], ar).then_inc(ar_dma, 16)
            sp.dma_start(b3_in[:], b3).then_inc(b3_dma, 16)
            load_w2(0)
            sp.dma_start(slot("w3"), w3T).then_inc(w3_in, 16)
            sp.wait_ge(S["x_lo"], K)
            load_w2(1)
            sp.wait_ge(S["w1_lo"], K)
            load_w2(2)
            sp.wait_ge(S["w2_lo"], K)
            load_w2(3)
            sp.wait_ge(S["w3_lo"], 2)
            for k in range(K):
                sp.dma_start(slot("x1")[:, k], xT[1, k]).then_inc(x_in[k], 16)
            for b in (4, 5, 6):
                sp.wait_ge(S["w2_lo"], K * (b - 3 + 1))
                load_w2(b)

            def store(b):
                sp.wait_ge(res_ok, b + 1)
                sp.dma_start(out[b], res[:, b % 2]).then_inc(out_done[b % 2], 16)

            for b in range(HB - 1):
                store(b)
            sp.wait_ge(S["x_lo"], 2 * K)
            load_w2(7)
            for b in range(HB - 1, B):
                store(b)
            for i in range(2):
                sp.wait_ge(out_done[i], 16 * (B // 2))

        @block.gpsimd
        def _(pool):
            pool.memset(eye[:], 0.0).then_inc(eye_zero, 1)
            pool.wait_ge(eye_zero, 1)
            pool.affine_select(out=eye[:], in_=eye[:], compare_op=ALU.not_equal, fill=1.0, base=0,
                               pattern=[[-1, P]], channel_multiplier=1).then_inc(eye_ok, 1)
            pool.wait_ge(ids_in, 16)
            for i in (I_ROW0, I_ROW1):
                pool.tensor_scalar(rows[:, i:i + 1], ids[:, i:i + 1], float(R), ids[:, I_RANK:I_RANK + 1],
                                   ALU.mult, ALU.add).then_inc(rows_ok, 1)
            pool.wait_ge(rows_ok, 2)
            for g, table, i, s in ((g0, gather0, I_ROW0, g0_in), (g1, gather1, I_ROW1, g1_in)):
                pool.indirect_dma_start(out=g[:].rearrange("p a d -> p (a d)"), out_offset=None, in_=table,
                                        in_offset=bass.IndirectOffsetOnAxis(ap=rows[:, i:i + 1], axis=0),
                                        bounds_check=table.shape[0] - 1).then_inc(s, 16)
            pool.wait_ge(eye_ok, 1)

            def add_eye(name, s):
                d = diagonal(slot(name))
                pool.tensor_tensor(d, d, ident[:, None, :].to_broadcast([P, K, P]), ALU.add).then_inc(s, 1)

            pool.wait_ge(w2_in[0], 16)
            add_eye("w2_0", w2_eye)
            pool.wait_ge(w3_in, 16)
            add_eye("w3", w3_eye)
            for b in range(1, B):
                pool.wait_ge(w2_in[b % 4], 16 * (b // 4 + 1))
                add_eye(f"w2_{b}", w2_eye)
                if b == 2:
                    for c in range(2):
                        s = slice(2 * c, 2 * c + 2)
                        pool.wait_ge(S["w3_hi"], c + 1)
                        pool.tensor_tensor(w3_lo[:, s], slot("w3")[:, s], w3_hi[:, s].bitcast(F32), ALU.subtract) \
                            .then_inc(S["w3_lo"], 1)

        @block.scalar
        def _(act):
            def hi(dst, src, name, parts=1):
                return nc.scalar.copy(dst, src).then_inc(S[name + "_hi"], parts)

            def split_x(h, k):
                act.wait_ge(x_in[k], 16 * (h + 1))
                if h:
                    act.wait_ge(l1x_mm, 1)
                hi(x_hi[:, k], slot(f"x{h}")[:, k], "x")

            def split_w1(k):
                act.wait_ge(w1_eye, k + 1)
                hi(w1_hi[:, k], slot("w1")[:, k], "w1")

            def split_w2(b, k0, k1):
                act.wait_ge(w2_eye, b + 1)
                if b >= 2:
                    act.wait_ge(x3_mm, b - 1)
                hi(w2_hi[:, b % 2, k0:k1], slot(f"w2_{b}")[:, k0:k1], "w2", k1 - k0)

            def split_w3(c):
                act.wait_ge(w3_eye, 1)
                hi(w3_hi[:, 2 * c:2 * c + 2], slot("w3")[:, 2 * c:2 * c + 2], "w3")

            act.wait_ge(warm_ok, 1)
            nc.scalar.activation(ex[:, 0], x3[:, 0, 0:1], ACT.Exp).then_inc(warm_ok, 1)
            for k in range(K):
                split_w1(k)
                split_x(0, k)
            act.wait_ge(a0t_mm, 1)
            hi(a0_hi[:], bank[A0T_BANK][:], "a0")
            act.wait_ge(a1t_mm, 1)
            hi(a1_hi[:], bank[A1T_BANK][:], "a1")
            act.wait_ge(b0t_mm, 1)
            b0t = bank[B0T_BANK][:].rearrange("p (k c) -> p k c", k=K)
            hi(dn_hi[:, :, 0, 0:HR], b0t[:, :, 0:HR], "dnu")
            hi(dn_hi[:, :, 1, HR:P], b0t[:, :, HR:P], "dnu")
            hi(b0_hi[:], g0[:, 0], "b0")
            act.wait_ge(S["a1_lo"], 1)
            nc.scalar.copy(a1[:], bank[A1T_BANK][:]).then_inc(a1_ok, 1)
            act.wait_ge(gm_ok, 1)
            hi(g_hi[:], gm[:], "g")
            act.wait_ge(ar_dma, 16)
            hi(ar_hi[:], ar_in[:], "ar")
            act.wait_ge(b3_dma, 16)
            hi(b3_hi[:], b3_in[:], "b3")
            act.wait_ge(a1t_mm, 1)
            nc.scalar.copy(g1[HR:P, 0], g1[HR:P, 1]).then_inc(up_ok, 1)
            split_w2(0, 0, 2)
            act.wait_ge(a1g_ok, 1)
            hi(dn_hi[:, :, 0, HR:P], a1[:, :, HR:P], "dnv")
            hi(dn_hi[:, :, 1, 0:HR], a1[:, :, 0:HR], "dnv")
            split_w3(0)
            act.wait_ge(aw_mm, 1)
            act.wait_ge(up_ok, 1)
            nc.scalar.copy(g1[0:HR, 0], bank[AW_BANK][0:HR, :]).then_inc(up_ok, 1)
            nc.scalar.copy(g1[HR:P, 1], bank[AW_BANK][HR:P, :]).then_inc(up_ok, 1)
            act.wait_ge(up_ok, 3)
            hi(up_hi[:], g1[:], "up")
            split_w2(0, 2, 4)

            for h in range(2):
                b0 = HB * h
                act.wait_ge(uv_ok, h + 1)
                if h:
                    act.wait_ge(x2_mm, K)
                hi(uv_hi[:], uv[:], "uv")
                if h == 0:
                    split_w3(1)
                    split_w2(1, 0, 2)
                for o in range(K):
                    act.wait_ge(x2_mm, K * h + o + 1)
                    hi(x2_hi[:, o], bank[L1_BANK + o][:], "x2")
                if h == 0:
                    split_w2(1, 2, 4)

                def evacuate_x3(b):
                    act.wait_ge(x3_mm, b + 1)
                    if b >= 2:
                        act.wait_ge(x3t_mm, b - 1)
                    nc.scalar.copy(x3[:, b % 2], bank[X3_BANK + b % 2][:]).then_inc(x3_ok, 1)

                def split_x3t(b):
                    act.wait_ge(x3t_mm, b + 1)
                    if b >= 2:
                        act.wait_ge(out_mm, b - 1)
                    hi(x3_hi[:, b % 2].rearrange("p k t -> p (k t)"), bank[X3T_BANK][:], "x3t")

                def exp_gap(b):
                    act.wait_ge(gap_ok, b + 1)
                    nc.scalar.activation(ex[:, b % 2], gap[:, b % 2], ACT.Exp).then_inc(ex_ok, 1)

                evacuate_x3(b0)
                split_w2(b0 + 2, 0, 1)
                split_x3t(b0)
                evacuate_x3(b0 + 1)
                split_w2(b0 + 2, 1, 2)
                exp_gap(b0)
                split_x3t(b0 + 1)
                split_w2(b0 + 2, 2, 4)
                for j in range(HB):
                    b = b0 + j
                    if j in (1, 2):
                        split_x3t(b + 1)
                    if h == 0 and j == 1:
                        split_x(1, 0)
                        split_x(1, 1)
                    act.wait_ge(hgt_mm, b + 1)
                    hi(hg_hi[:, b % 2], bank[HGT_BANK][:, 0:P], "hgt")
                    if j == 0:
                        split_w2(b0 + 3, 0, 2)
                        split_w2(b0 + 3, 2, 4)
                    if h == 0 and j == 1:
                        split_x(1, 2)
                        split_x(1, 3)
                    if j < 2:
                        evacuate_x3(b + 2)
                    if j < 3:
                        exp_gap(b + 1)
                    act.wait_ge(out_mm, b + 1)
                    if b >= 2:
                        act.wait_ge(out_done[b % 2], 16 * (b // 2))
                    nc.scalar.copy(res[:, b % 2], bank[OUT_BANK + b % 2][:]).then_inc(res_ok, 1)
                    if h == 0 and j >= 2:
                        split_w2(b + 2, 0, 2)
                        split_w2(b + 2, 2, 4)

        @block.vector
        def _(dve):
            links = [0]

            def link(ins):
                links[0] += 1
                ins.then_inc(chain, 1)
                dve.wait_ge(chain, links[0])

            count = {}

            def lo(dst, src, hi_part, name, parts=1):
                count[name] = count.get(name, 0) + parts
                dve.wait_ge(S[name + "_hi"], count[name])
                return dve.tensor_tensor(dst, src, hi_part.bitcast(F32), ALU.subtract).then_inc(S[name + "_lo"], parts)

            def split_x(h, k):
                lo(x_lo[:, k], slot(f"x{h}")[:, k], x_hi[:, k], "x")

            def split_w1(k):
                lo(w1_lo[:, k], slot("w1")[:, k], w1_hi[:, k], "w1")

            def split_w2(b, k0, k1):
                lo(w2_lo[:, b % 2, k0:k1], slot(f"w2_{b}")[:, k0:k1], w2_hi[:, b % 2, k0:k1], "w2", k1 - k0)

            dve.memset(x3[:, 0, 0:D // 2], 0.0).then_inc(warm_ok, 1)
            dve.wait_ge(eye_ok, 1)
            for k in range(K):
                dve.wait_ge(w1_in[k], 16)
                d = slot("w1")[:, k, k * P:(k + 1) * P]
                dve.tensor_tensor(d, d, ident, ALU.add).then_inc(w1_eye, 1)
                split_w1(k)
                split_x(0, k)
            lo(a0_lo[:], bank[A0T_BANK][:].rearrange("p (k c) -> p k c", k=K), a0_hi[:], "a0")
            lo(a1_lo[:], bank[A1T_BANK][:].rearrange("p (k c) -> p k c", k=K), a1_hi[:], "a1")
            b0t = bank[B0T_BANK][:].rearrange("p (k c) -> p k c", k=K)
            dve.wait_ge(S["dnu_hi"], 2)
            lo(dn_lo[:, :, 0, 0:HR], b0t[:, :, 0:HR], dn_hi[:, :, 0, 0:HR], "dnu")
            lo(dn_lo[:, :, 1, HR:P], b0t[:, :, HR:P], dn_hi[:, :, 1, HR:P], "dnu")
            lo(b0_lo[:], g0[:, 0], b0_hi[:], "b0")
            dve.wait_ge(cst_in, 16)
            dve.wait_ge(g_mm, 1)
            dve.tensor_tensor(gm[:], bank[G_BANK][:, 0:P], cst[:, C_GMASK:C_GMASK + P], ALU.mult).then_inc(gm_ok, 1)
            lo(g_lo[:], gm[:], g_hi[:], "g")
            lo(ar_lo[:], ar_in[:], ar_hi[:], "ar")
            lo(b3_lo[:], b3_in[:], b3_hi[:], "b3")
            dve.wait_ge(bg_mm, 1)
            dve.wait_ge(a1_ok, 1)
            dve.tensor_tensor(a1[:], bank[BG_BANK][:].rearrange("p (k c) -> p k c", k=K), a1[:], ALU.add) \
               .then_inc(a1g_ok, 1)
            lo(dn_lo[:, :, 0, HR:P], a1[:, :, HR:P], dn_hi[:, :, 0, HR:P], "dnv")
            lo(dn_lo[:, :, 1, 0:HR], a1[:, :, 0:HR], dn_hi[:, :, 1, 0:HR], "dnv")
            ids3 = ids[:, I_LANG:I_LANG + B].rearrange("p (b e) -> p b e", e=1).to_broadcast([P, B, E])
            link(dve.tensor_tensor(onehot[:], ids3, iota[:, None, :].to_broadcast([P, B, E]), ALU.is_equal))
            dve.tensor_scalar(bias[:], onehot[:], LANG_BIAS / P, None, ALU.mult).then_inc(bias_ok, 1)
            dve.tensor_scalar(ones[:], ident, 0.0, 1.0, ALU.mult, ALU.add).then_inc(bias_ok, 1)
            split_w2(0, 0, 2)

            for h in range(2):
                b0 = HB * h
                dve.wait_ge(uv_mm, h + 1)
                mask = cst[:, C_UVMASK:C_UVMASK + HB].rearrange("p (j t) -> p j t", t=1).to_broadcast([P, HB, P])
                dve.tensor_tensor(uv[:].rearrange("p (j t) -> p j t", j=HB),
                                  bank[UV_BANK][:].rearrange("p (j t) -> p j t", j=HB), mask, ALU.mult) \
                   .then_inc(uv_ok, 1)
                if h == 0:
                    lo(up_lo[:], g1[:], up_hi[:], "up")
                lo(uv_lo[:], uv[:], uv_hi[:], "uv")
                if h == 0:
                    split_w2(0, 2, 4)
                for o in range(K):
                    lo(x2_lo[:, o], bank[L1_BANK + o][:], x2_hi[:, o], "x2")
                if h == 0:
                    split_w2(1, 0, 2)
                    split_w2(1, 2, 4)

                def split_x3t(b):
                    lo(x3_lo[:, b % 2].rearrange("p k t -> p (k t)"), bank[X3T_BANK][:],
                       x3_hi[:, b % 2].rearrange("p k t -> p (k t)"), "x3t")

                def route(b):
                    q = b % 2
                    logits = bank[AR_BANK][:, E * R:AR]
                    dve.wait_ge(ar_mm, b + 1)
                    link(dve.max(top[:, q], logits))
                    dve.tensor_tensor(gap[:, q], top[:, q, 1:2], top[:, q, 0:1], ALU.subtract).then_inc(gap_ok, 1)
                    link(dve.max_index(topi[:, q], top[:, q], logits))
                    at = topi[:, q, 0:2].rearrange("p (s e) -> p s e", e=1).to_broadcast([P, 2, E])
                    dve.tensor_tensor(hot[:, q], at, iota[:, None, :].to_broadcast([P, 2, E]), ALU.is_equal) \
                       .then_inc(chain, 1)
                    links[0] += 1

                def gates(b):
                    q = b % 2
                    dve.wait_ge(ex_ok, b + 1)
                    dve.wait_ge(chain, links[0])
                    dve.tensor_scalar(rden[:, q, 0:1], ex[:, q], 0.5, 0.5, ALU.mult, ALU.add).then_inc(chain, 1)
                    dve.scalar_tensor_tensor(out=gate[:, q], in0=hot[:, q, 1], scalar=ex[:, q, 0:1], in1=hot[:, q, 0],
                                             op0=ALU.mult, op1=ALU.add).then_inc(chain, 1)
                    links[0] += 2
                    dve.wait_ge(chain, links[0])
                    link(dve.reciprocal(rden[:, q, 1:2], rden[:, q, 0:1]))
                    g = gate[:, q].rearrange("p (e r) -> p e r", r=1).to_broadcast([P, E, R])
                    dve.scalar_tensor_tensor(out=hg[:, q].rearrange("p (e r) -> p e r", e=E),
                                             in0=bank[AR_BANK][:, 0:E * R].rearrange("p (e r) -> p e r", e=E),
                                             scalar=rden[:, q, 1:2], in1=g, op0=ALU.mult, op1=ALU.mult) \
                       .then_inc(hg_ok, 1)

                split_w2(b0 + 2, 0, 1)
                split_x3t(b0)
                split_w2(b0 + 2, 1, 2)
                route(b0)
                split_x3t(b0 + 1)
                gates(b0)
                split_w2(b0 + 2, 2, 4)
                for j in range(HB):
                    b = b0 + j
                    if j in (1, 2):
                        split_x3t(b + 1)
                    if h == 0 and j == 1:
                        split_x(1, 0)
                        split_x(1, 1)
                    lo(hg_lo[:, b % 2], bank[HGT_BANK][:, 0:P], hg_hi[:, b % 2], "hgt")
                    if j == 0:
                        split_w2(b0 + 3, 0, 2)
                        split_w2(b0 + 3, 2, 4)
                    if h == 0 and j == 1:
                        split_x(1, 2)
                        split_x(1, 3)
                    if j < 3:
                        route(b + 1)
                        gates(b + 1)
                    if h == 0 and j >= 2:
                        split_w2(b + 2, 0, 2)
                        split_w2(b + 2, 2, 4)

        @block.tensor
        def _(pe):
            def product(out, lhs, rhs, first=True, last=True, between=lambda i: None):
                nc.tensor.matmul(out, lhs[0], rhs[0], start=first, stop=False)
                between(0)
                nc.tensor.matmul(out, lhs[1], rhs[0], start=False, stop=False)
                between(1)
                end = nc.tensor.matmul(out, lhs[0], rhs[1], start=False, stop=last)
                between(2)
                return end

            def layer1_first():
                for (w, x), ready in (((w1_hi, x_hi), ("w1_hi", "x_hi")), ((w1_lo, x_hi), ("w1_lo",)),
                                      ((w1_hi, x_lo), ("x_lo",))):
                    for n in ready:
                        pe.wait_ge(S[n], 1)
                    for o in range(K):
                        nc.tensor.matmul(bank[L1_BANK + o][:], w[:, 0, o * P:(o + 1) * P], x[:, 0],
                                         start=(ready[0] == "w1_hi"), stop=False)

            def layer1(h, k, chunks=range(K)):
                pe.wait_ge(S["x_lo"], K * h + k + 1)
                pe.wait_ge(S["w1_lo"], k + 1)
                for o in chunks:
                    c = slice(o * P, (o + 1) * P)
                    last = product(bank[L1_BANK + o][:], (w1_hi[:, k, c], w1_lo[:, k, c]), (x_hi[:, k], x_lo[:, k]),
                                   first=(k == 0), last=False)
                return last

            def down(h):
                pe.wait_ge(S["x_lo"], K * (h + 1))
                pe.wait_ge(S["dnu_lo"], 2)
                pe.wait_ge(S["dnv_lo"], 2)
                for k in range(K):
                    last = product(bank[UV_BANK][:], (dn_hi[:, k, h], dn_lo[:, k, h]), (x_hi[:, k], x_lo[:, k]),
                                   first=(k == 0), last=(k == K - 1))
                last.then_inc(uv_mm, 1)

            def up(h):
                pe.wait_ge(S["uv_lo"], h + 1)
                pe.wait_ge(S["up_lo"], 1)
                for o in range(K):
                    c = slice(o * P, (o + 1) * P)
                    product(bank[L1_BANK + o][:], (up_hi[:, h, c], up_lo[:, h, c]), (uv_hi[:], uv_lo[:]),
                            first=False).then_inc(x2_mm, 1)

            def transposes(dst, src):
                for k in range(K):
                    last = nc.tensor.transpose(dst[:, k * P:(k + 1) * P], src[:, k * P:(k + 1) * P], ident)
                return last

            def layer2(b, chunks=range(K), between=lambda i: None):
                j = b % HB
                t = slice(j * P, (j + 1) * P)
                for k in chunks:
                    pe.wait_ge(S["x2_lo"], K * (b // HB) + (k + 1 if j == 0 else K))
                    pe.wait_ge(S["w2_lo"], K * b + k + 1)
                    if k == 0 and j >= 2:
                        pe.wait_ge(x3_ok, b - 1)
                    last = product(bank[X3_BANK + b % 2][:], (x2_hi[:, k, t], x2_lo[:, k, t]),
                                   (w2_hi[:, b % 2, k], w2_lo[:, b % 2, k]), first=(k == 0), last=(k == K - 1),
                                   between=lambda i: between(3 * k + i))
                if K - 1 in chunks:
                    last.then_inc(x3_mm, 1)

            def transpose_x3(b):
                pe.wait_ge(x3_ok, b + 1)
                if b % HB:
                    pe.wait_ge(S["x3t_lo"], b)
                transposes(bank[X3T_BANK], x3[:, b % 2]).then_inc(x3t_mm, 1)

            def down3(b, step):
                q = b % 2
                if step == 0:
                    pe.wait_ge(S["x3t_lo"], b + 1)
                    pe.wait_ge(S["ar_lo"], 1)
                    pe.wait_ge(bias_ok, 2)
                    if b % HB:
                        pe.wait_ge(hg_ok, b)
                if step == 3 * K:
                    nc.tensor.matmul(bank[AR_BANK][:, E * R:AR], ones[:], bias[:, b], start=False, stop=True) \
                      .then_inc(ar_mm, 1)
                    return
                k, i = divmod(step, 3)
                lhs, rhs = ((x3_hi, ar_hi), (x3_lo, ar_hi), (x3_hi, ar_lo))[i]
                nc.tensor.matmul(bank[AR_BANK][:, 0:AR], lhs[:, q, k], rhs[:, k], start=(step == 0), stop=False)

            def layer3(b, chunks, between=lambda i: None):
                q = b % 2
                if 0 in chunks:
                    pe.wait_ge(S["x3t_lo"], b + 1)
                    pe.wait_ge(S["w3_lo"], 2)
                    if b >= 2:
                        pe.wait_ge(res_ok, b - 1)
                for k in chunks:
                    product(bank[OUT_BANK + q][:], (x3_hi[:, q, k], x3_lo[:, q, k]), (w3_hi[:, k], w3_lo[:, k]),
                            first=(k == 0), last=False, between=lambda i: between(3 * k + i))

            def transpose_hg(b):
                pe.wait_ge(hg_ok, b + 1)
                if b:
                    pe.wait_ge(S["hgt_lo"], b)
                nc.tensor.transpose(bank[HGT_BANK][:, 0:P], hg[:, b % 2], ident).then_inc(hgt_mm, 1)

            def up3(b):
                q = b % 2
                pe.wait_ge(S["hgt_lo"], b + 1)
                pe.wait_ge(S["b3_lo"], 1)
                product(bank[OUT_BANK + q][:], (hg_hi[:, q], hg_lo[:, q]), (b3_hi[:], b3_lo[:]), first=False) \
                    .then_inc(out_mm, 1)

            pe.wait_ge(warm_ok, 1)
            for _ in range(WARM_UP):
                nc.tensor.matmul(bank[G_BANK][:], warm[:, 0:P], warm, start=True, stop=True)
            layer1_first()
            layer1(0, 1)
            pe.wait_ge(g0_in, 16)
            transposes(bank[A0T_BANK], g0[:, 1]).then_inc(a0t_mm, 1)
            pe.wait_ge(g1_in, 16)
            transposes(bank[A1T_BANK], g1[:, 0]).then_inc(a1t_mm, 1)
            transposes(bank[B0T_BANK], g0[:, 0]).then_inc(b0t_mm, 1)
            layer1(0, 2, range(2))
            pe.wait_ge(S["a0_lo"], 1)
            pe.wait_ge(S["a1_lo"], 1)
            for k in range(K):
                last = product(bank[G_BANK][:, 0:P], (a0_hi[:, k], a0_lo[:, k]), (a1_hi[:, k], a1_lo[:, k]),
                               first=(k == 0), last=(k == K - 1))
            last.then_inc(g_mm, 1)
            layer1(0, 2, range(2, K))
            pe.wait_ge(S["g_lo"], 1)
            pe.wait_ge(S["b0_lo"], 1)
            pe.wait_ge(S["dnu_lo"], 2)
            for k in range(K):
                c = slice(k * P, (k + 1) * P)
                last = product(bank[BG_BANK][:, c], (b0_hi[:, c], b0_lo[:, c]), (g_hi[:], g_lo[:]))
            last.then_inc(bg_mm, 1)
            pe.wait_ge(S["w1_lo"], K)
            for k in range(K):
                last = product(bank[AW_BANK][:], (a0_hi[:, k], a0_lo[:, k]), (w1_hi[:, k], w1_lo[:, k]),
                               first=(k == 0), last=(k == K - 1))
            last.then_inc(aw_mm, 1)
            down(0)
            layer1(0, 3).then_inc(l1x_mm, 1)
            up(0)

            for h in range(2):
                b0 = HB * h
                layer2(b0)
                layer2(b0 + 1, range(2))
                transpose_x3(b0)
                layer2(b0 + 1, range(2, K))
                layer2(b0 + 2, [0])
                for step in range(3 * K + 1):
                    down3(b0, step)
                transpose_x3(b0 + 1)
                layer3(b0, range(K))
                transpose_hg(b0)
                for step in range(3):
                    down3(b0 + 1, step)
                layer2(b0 + 2, range(1, K), between=lambda i: down3(b0 + 1, i))
                down3(b0 + 1, 3 * K)
                up3(b0)
                transpose_x3(b0 + 2)
                layer3(b0 + 1, range(3))
                transpose_hg(b0 + 1)
                layer3(b0 + 1, [3])
                layer2(b0 + 3, between=lambda i: down3(b0 + 2, i))
                down3(b0 + 2, 3 * K)
                up3(b0 + 1)
                transpose_x3(b0 + 3)
                layer3(b0 + 2, range(2))

                def two_steps(i):
                    for step in (2 * (i - 6), 2 * (i - 6) + 1):
                        down3(b0 + 3, step)

                layer3(b0 + 2, [2], two_steps)
                transpose_hg(b0 + 2)
                layer3(b0 + 2, [3], two_steps)
                down3(b0 + 3, 3 * K)
                up3(b0 + 2)
                layer3(b0 + 3, range(3))
                transpose_hg(b0 + 3)
                layer3(b0 + 3, [3])
                if h == 0:
                    down(1)
                up3(b0 + 3)
                if h == 0:
                    for k in range(K):
                        layer1(1, k)
                    up(1)


_OUT = (B, P, D)


def kernel(**inputs):
    import numpy as np
    import concourse.bacc as bacc
    from concourse.bass_utils import run_bass_kernel_spmd

    a = {n: np.asarray(v) for n, v in inputs.items()}
    part = np.arange(P)
    consts = np.zeros((P, C_COLS), np.float32)
    consts[:, C_GMASK:C_GMASK + P] = part[:, None] // R == (part[None, :] // R + HB) % B
    consts[:, C_UVMASK:C_UVMASK + HB] = (part[:, None] % HR) // R == np.arange(HB)[None, :]
    consts[:, C_IOTA:C_IOTA + E] = np.arange(E)
    id0, id1, id3 = (a[n].reshape(B) for n in ("itok_B_3_7", "itok_B_0_15", "itok_B_0_7"))
    spread = lambda v: np.broadcast_to(v[None, :], (P, B))
    ints = np.concatenate([np.repeat(id0, R)[:, None], np.repeat(np.concatenate([id1[HB:], id1[:HB]]), R)[:, None],
                           (part % R).astype(id0.dtype)[:, None], spread(id3), spread(id0)], 1)
    t = np.transpose
    arrays = {
        "consts": consts,
        "ints": ints,
        "xT": t(a["x"].reshape(2, T, K, P), (0, 2, 3, 1)),
        "w1": a["L1_cond_W"].reshape(K, P, D),
        "gather0": np.concatenate([a["L0_cond_B"], t(a["L0_cond_A"], (0, 2, 1))], 2).reshape(-1, 2 * D),
        "gather1": np.concatenate([t(a["L1_cond_lora_A"], (0, 2, 1)), a["L1_cond_lora_B"]], 2).reshape(-1, 2 * D),
        "w2T": t(a["L2_cond_weight"].reshape(E, D, K, P), (0, 3, 2, 1)),
        "w3T": t(a["L3_cond_W"].reshape(D, K, P), (2, 1, 0)),
        "ar": t(np.concatenate([a["L3_cond_A"].reshape(E * R, D), a["L3_cond_Wr"]], 0).reshape(AR, K, P), (2, 1, 0)),
        "b3": t(a["L3_cond_B"], (0, 2, 1)).reshape(E * R, D),
    }
    arrays = {n: np.ascontiguousarray(v) for n, v in arrays.items()}
    nc = bacc.Bacc("TRN2", target_bir_lowering=False, num_devices=1)
    args = [nc.dram_tensor(n, v.shape, mybir.dt.from_np(v.dtype), kind="ExternalInput").ap() for n, v in arrays.items()]
    args.append(nc.dram_tensor("out", _OUT, F32, kind="ExternalOutput").ap())
    cond_resid_kernel(nc, *args)
    r = run_bass_kernel_spmd(nc, [arrays], core_ids=[0])
    return r.results[0]["out"]
```

```python
from contextlib import ExitStack

import concourse.bass as bass
from concourse import mybir

F32 = mybir.dt.float32
F32R = mybir.dt.float32r
BF16 = mybir.dt.bfloat16
I32 = mybir.dt.int32
U32 = mybir.dt.uint32
ALU = mybir.AluOpType
ACT = mybir.ActivationFunctionType

P = 128
D = 512
K = D // P
B = 8
HB = B // 2
T = HB * P
R = 16
E = 8
HR = HB * R
AR = E * R + E
H = D // 2
LANG_BIAS = 5.0
WARM_UP = 10
STAGES = 4

C_GMASK = 0
C_UVMASK = C_GMASK + P
C_IOTA = C_UVMASK + HB
C_COLS = C_IOTA + E
I_ROW0, I_ROW1, I_RANK, I_LANG, I_W2 = 0, 1, 2, 3, 3 + B
I_COLS = 3 + 2 * B

LOADS = ["x0", "w1", "w2_0", "w3", "w2_1", "w2_2", "w2_3", "x1", "w2_4", "w2_5", "w2_6", "w2_7"]
SLOT = {name: i % STAGES for i, name in enumerate(LOADS)}


def cond_resid_kernel(nc, consts, ints, xT, w1, gather0, gather1, w2T, w3T, ar, b3, out):
    with ExitStack() as ctx:
        def sb(name, shape, dt=F32):
            return ctx.enter_context(nc.sbuf_tensor(name, shape, dt))

        def sem(name):
            return ctx.enter_context(nc.semaphore(name))

        cst = sb("cst", [P, C_COLS])
        eye = sb("eye", [P, P])
        ids = sb("ids", [P, I_COLS], I32)
        rows = sb("rows", [P, 2], U32)
        stage = sb("stage", [P, STAGES, K, D])
        x_hi, x_lo = sb("x_hi", [P, K, T], F32R), sb("x_lo", [P, K, T], F32R)
        w1_hi, w1_lo = sb("w1_hi", [P, K, D], F32R), sb("w1_lo", [P, K, D], F32R)
        w2_hi, w2_lo = sb("w2_hi", [P, 2, K, D], F32R), sb("w2_lo", [P, 2, K, D], F32R)
        w3_hi, w3_lo = sb("w3_hi", [P, K, D + AR], F32R), sb("w3_lo", [P, K, D + AR], F32R)
        ar_in = sb("ar_in", [P, K, AR])
        b3_in = sb("b3_in", [P, D])
        b3_hi, b3_lo = sb("b3_hi", [P, D], F32R), sb("b3_lo", [P, D], F32R)
        g0 = sb("g0", [P, 2, D])
        g1 = sb("g1", [P, 2, D])
        a0_hi, a0_lo = sb("a0_hi", [P, K, P], F32R), sb("a0_lo", [P, K, P], F32R)
        a1 = sb("a1", [P, K, P])
        a1_hi, a1_lo = sb("a1_hi", [P, K, P], F32R), sb("a1_lo", [P, K, P], F32R)
        b0_hi, b0_lo = sb("b0_hi", [P, D], F32R), sb("b0_lo", [P, D], F32R)
        gm = sb("gm", [P, P])
        g_hi, g_lo = sb("g_hi", [P, P], F32R), sb("g_lo", [P, P], F32R)
        dn_hi, dn_lo = sb("dn_hi", [P, K, 2, P], F32R), sb("dn_lo", [P, K, 2, P], F32R)
        up_hi, up_lo = sb("up_hi", [P, 2, D], F32R), sb("up_lo", [P, 2, D], F32R)
        uv = sb("uv", [P, T])
        uv_hi, uv_lo = sb("uv_hi", [P, T], F32R), sb("uv_lo", [P, T], F32R)
        x2_hi, x2_lo = sb("x2_hi", [P, K, T], F32R), sb("x2_lo", [P, K, T], F32R)
        x3 = sb("x3", [P, 2, D])
        x3_hi, x3_lo = sb("x3_hi", [P, 2, K, P], F32R), sb("x3_lo", [P, 2, K, P], F32R)
        onehot = sb("onehot", [P, B, E])
        bias = sb("bias", [P, B, E])
        logits = sb("logits", [P, 2, E])
        top = sb("top", [P, 2, 8])
        topi = sb("topi", [P, 2, 8], U32)
        hot = sb("hot", [P, 2, 2, E])
        gap = sb("gap", [P, 2, 1])
        ex = sb("ex", [P, 2, 1])
        rden = sb("rden", [P, 2, 2])
        gate = sb("gate", [P, 2, E])
        hg = sb("hg", [P, 2, P])
        hg_hi, hg_lo = sb("hg_hi", [P, 2, P], F32R), sb("hg_lo", [P, 2, P], F32R)
        res = sb("res", [P, 2, D])
        warm = x3[:, 0, 0:D // 2].bitcast(BF16)

        bank = [ctx.enter_context(nc.psum_tensor(f"bank{i}", [P, D], F32)) for i in range(4)]
        pair = [ctx.enter_context(nc.psum_tensor(f"pair{q}", [P, 2, D], F32)) for q in range(2)]
        L1_BANK, X3_BANK, X3T_BANK, HGT_BANK = 0, 0, 2, 3
        a0t_bank, a1t_bank, b0t_bank, g_bank = pair[0][:, 0], pair[0][:, 1], pair[1][:, 0], pair[1][:, 1]
        aw_bank, uv_bank, bg_bank = a0t_bank, a1t_bank, b0t_bank
        up_high = bank[HGT_BANK][:, P:P + H]

        cst_in, ids_in = sem("cst_in"), sem("ids_in")
        x_in = [sem(f"x_in{k}") for k in range(K)]
        w1_in = [sem(f"w1_in{k}") for k in range(K)]
        w2_in = [sem(f"w2_in{i}") for i in range(4)]
        w3_in, ar_dma, b3_dma = sem("w3_in"), sem("ar_dma"), sem("b3_dma")
        g0_in, g1_in = sem("g0_in"), sem("g1_in")
        out_done = [sem(f"out_done{i}") for i in range(2)]
        w1_eye, w2_eye, w3_eye, rows_ok = sem("w1_eye"), sem("w2_eye"), sem("w3_eye"), sem("rows_ok")
        eye_zero, eye_ok = sem("eye_zero"), sem("eye_ok")
        S = {}
        for n in ("x", "w1", "w2", "w3", "ar", "b3", "a0", "a1", "b0", "g", "dnu", "dnv", "up", "uv", "x2",
                  "x3t", "hgt"):
            S[n + "_hi"], S[n + "_lo"] = sem(n + "_hi_ok"), sem(n + "_lo_ok")
        a1_ok, gm_ok, a1g_ok, up_ok = (sem(n) for n in ("a1_ok", "gm_ok", "a1g_ok", "up_ok"))
        uv_ok, x3_ok = sem("uv_ok"), sem("x3_ok")
        low_ok, high_ok, base_ok = sem("low_ok"), sem("high_ok"), sem("base_ok")
        gap_ok, ex_ok, hg_ok, chain = (sem(n) for n in ("gap_ok", "ex_ok", "hg_ok", "chain"))
        warm_ok = sem("warm_ok")
        a0t_mm, a1t_mm, b0t_mm, g_mm, bg_mm, aw_mm = (sem(n) for n in
                                                      ("a0t_mm", "a1t_mm", "b0t_mm", "g_mm", "bg_mm", "aw_mm"))
        uv_mm, l1x_mm, x2_mm, x3_mm, x3t_mm = (sem(n) for n in ("uv_mm", "l1x_mm", "x2_mm", "x3_mm", "x3t_mm"))
        ar_mm, hgt_mm, low_mm, high_mm = (sem(n) for n in ("ar_mm", "hgt_mm", "low_mm", "high_mm"))

        iota = cst[:, C_IOTA:C_IOTA + E]

        def slot(name):
            return stage[:, SLOT[name]]

        def diagonal(w):
            return bass.AP(w.tensor, w.offset, [list(w.ap[0]), [D + P, K], [1, P]])

        ident = eye[:]

        block = ctx.enter_context(nc.Block())

        @block.sync
        def _(sp):
            for k in range(K):
                sp.dma_start(slot("w1")[:, k], w1[k]).then_inc(w1_in[k], 16)
                if k == 0:
                    sp.dma_start(ids[:], ints).then_inc(ids_in, 16)
                sp.dma_start(slot("x0")[:, k], xT[0, k]).then_inc(x_in[k], 16)
            sp.dma_start(cst[:], consts).then_inc(cst_in, 16)
            sp.wait_ge(ids_in, 16)

            def load_w2(b):
                adapter = sp.value_load(ids[0:1, I_W2 + b:I_W2 + b + 1], min_val=0, max_val=E - 1)
                sp.dma_start(slot(f"w2_{b}"), w2T[bass.DynSlice(adapter, 1)].rearrange("e p k o -> p (e k) o")) \
                    .then_inc(w2_in[b % 4], 16)

            sp.wait_ge(g0_in, 16)
            sp.dma_start(ar_in[:], ar).then_inc(ar_dma, 16)
            sp.dma_start(b3_in[:], b3).then_inc(b3_dma, 16)
            load_w2(0)
            sp.dma_start(slot("w3"), w3T).then_inc(w3_in, 16)
            sp.wait_ge(S["x_lo"], K)
            load_w2(1)
            sp.wait_ge(S["w1_lo"], K)
            load_w2(2)
            sp.wait_ge(S["w2_lo"], K)
            load_w2(3)
            sp.wait_ge(S["w3_lo"], 2)
            for k in range(K):
                sp.dma_start(slot("x1")[:, k], xT[1, k]).then_inc(x_in[k], 16)
            for b in (4, 5, 6):
                sp.wait_ge(S["w2_lo"], K * (b - 3 + 1))
                load_w2(b)

            def store(b):
                sp.wait_ge(low_ok, b + 1)
                sp.wait_ge(high_ok, b + 1)
                sp.dma_start(out[b], res[:, b % 2]).then_inc(out_done[b % 2], 16)

            for b in range(HB - 1):
                store(b)
            sp.wait_ge(S["x_lo"], 2 * K)
            load_w2(7)
            for b in range(HB - 1, B):
                store(b)
            for i in range(2):
                sp.wait_ge(out_done[i], 16 * (B // 2))

        @block.gpsimd
        def _(pool):
            pool.memset(eye[:], 0.0).then_inc(eye_zero, 1)
            pool.wait_ge(eye_zero, 1)
            pool.affine_select(out=eye[:], in_=eye[:], compare_op=ALU.not_equal, fill=1.0, base=0,
                               pattern=[[-1, P]], channel_multiplier=1).then_inc(eye_ok, 1)
            pool.wait_ge(ids_in, 16)
            for i in (I_ROW0, I_ROW1):
                pool.tensor_scalar(rows[:, i:i + 1], ids[:, i:i + 1], float(R), ids[:, I_RANK:I_RANK + 1],
                                   ALU.mult, ALU.add).then_inc(rows_ok, 1)
            pool.wait_ge(rows_ok, 2)
            for g, table, i, s in ((g0, gather0, I_ROW0, g0_in), (g1, gather1, I_ROW1, g1_in)):
                pool.indirect_dma_start(out=g[:].rearrange("p a d -> p (a d)"), out_offset=None, in_=table,
                                        in_offset=bass.IndirectOffsetOnAxis(ap=rows[:, i:i + 1], axis=0),
                                        bounds_check=table.shape[0] - 1).then_inc(s, 16)
            pool.wait_ge(eye_ok, 1)

            def add_eye(name, s):
                d = diagonal(slot(name))
                pool.tensor_tensor(d, d, ident[:, None, :].to_broadcast([P, K, P]), ALU.add).then_inc(s, 1)

            pool.wait_ge(w2_in[0], 16)
            add_eye("w2_0", w2_eye)
            pool.wait_ge(w3_in, 16)
            add_eye("w3", w3_eye)
            for b in range(1, B):
                pool.wait_ge(w2_in[b % 4], 16 * (b // 4 + 1))
                add_eye(f"w2_{b}", w2_eye)
                if b == 2:
                    for c in range(2):
                        s = slice(2 * c, 2 * c + 2)
                        pool.wait_ge(S["w3_hi"], c + 1)
                        pool.tensor_tensor(w3_lo[:, s, 0:D], slot("w3")[:, s], w3_hi[:, s, 0:D].bitcast(F32), ALU.subtract) \
                            .then_inc(S["w3_lo"], 1)

        @block.scalar
        def _(act):
            def hi(dst, src, name, parts=1):
                return nc.scalar.copy(dst, src).then_inc(S[name + "_hi"], parts)

            def split_x(h, k):
                act.wait_ge(x_in[k], 16 * (h + 1))
                if h:
                    act.wait_ge(l1x_mm, 1)
                hi(x_hi[:, k], slot(f"x{h}")[:, k], "x")

            def split_w1(k):
                act.wait_ge(w1_eye, k + 1)
                hi(w1_hi[:, k], slot("w1")[:, k], "w1")

            def split_w2(b, k0, k1):
                act.wait_ge(w2_eye, b + 1)
                if b >= 2:
                    act.wait_ge(x3_mm, b - 1)
                hi(w2_hi[:, b % 2, k0:k1], slot(f"w2_{b}")[:, k0:k1], "w2", k1 - k0)

            def split_w3(c):
                act.wait_ge(w3_eye, 1)
                hi(w3_hi[:, 2 * c:2 * c + 2, 0:D], slot("w3")[:, 2 * c:2 * c + 2], "w3")

            act.wait_ge(warm_ok, 1)
            nc.scalar.activation(ex[:, 0], x3[:, 0, 0:1], ACT.Exp).then_inc(warm_ok, 1)
            for k in range(K):
                split_w1(k)
                split_x(0, k)
            act.wait_ge(a0t_mm, 1)
            hi(a0_hi[:], a0t_bank, "a0")
            act.wait_ge(b0t_mm, 1)
            b0t = b0t_bank.rearrange("p (k c) -> p k c", k=K)
            hi(dn_hi[:, :, 0, 0:HR], b0t[:, :, 0:HR], "dnu")
            hi(dn_hi[:, :, 1, HR:P], b0t[:, :, HR:P], "dnu")
            act.wait_ge(a1t_mm, 1)
            hi(a1_hi[:], a1t_bank, "a1")
            hi(b0_hi[:], g0[:, 0], "b0")
            act.wait_ge(S["a1_lo"], 1)
            nc.scalar.copy(a1[:], a1t_bank).then_inc(a1_ok, 1)
            act.wait_ge(gm_ok, 1)
            hi(g_hi[:], gm[:], "g")
            act.wait_ge(ar_dma, 16)
            hi(w3_hi[:, :, D:D + AR], ar_in[:], "ar")
            act.wait_ge(b3_dma, 16)
            hi(b3_hi[:], b3_in[:], "b3")
            nc.scalar.copy(g1[HR:P, 0], g1[HR:P, 1]).then_inc(up_ok, 1)
            split_w2(0, 0, 2)
            act.wait_ge(a1g_ok, 1)
            hi(dn_hi[:, :, 0, HR:P], a1[:, :, HR:P], "dnv")
            hi(dn_hi[:, :, 1, 0:HR], a1[:, :, 0:HR], "dnv")
            split_w2(0, 2, 4)
            split_w3(0)
            act.wait_ge(aw_mm, 1)
            act.wait_ge(up_ok, 1)
            nc.scalar.copy(g1[0:HR, 0], aw_bank[0:HR, :]).then_inc(up_ok, 1)
            nc.scalar.copy(g1[HR:P, 1], aw_bank[HR:P, :]).then_inc(up_ok, 1)
            act.wait_ge(up_ok, 3)
            hi(up_hi[:], g1[:], "up", 2)

            for h in range(2):
                b0 = HB * h
                act.wait_ge(uv_ok, h + 1)
                if h:
                    act.wait_ge(x2_mm, K)
                hi(uv_hi[:], uv[:], "uv")
                if h == 0:
                    split_w3(1)
                    split_w2(1, 0, 2)
                for o in range(K):
                    act.wait_ge(x2_mm, K * h + o + 1)
                    hi(x2_hi[:, o], bank[L1_BANK + o][:], "x2")
                if h == 0:
                    split_w2(1, 2, 4)

                def evacuate_x3(b):
                    act.wait_ge(x3_mm, b + 1)
                    if b >= 2:
                        act.wait_ge(x3t_mm, b - 1)
                    nc.scalar.copy(x3[:, b % 2], bank[X3_BANK + b % 2][:]).then_inc(x3_ok, 1)

                def split_x3t(b):
                    act.wait_ge(x3t_mm, b + 1)
                    if b >= 2:
                        act.wait_ge(low_mm, b - 1)
                    hi(x3_hi[:, b % 2].rearrange("p k t -> p (k t)"), bank[X3T_BANK][:], "x3t")

                def exp_gap(b):
                    act.wait_ge(gap_ok, b + 1)
                    nc.scalar.activation(ex[:, b % 2], gap[:, b % 2], ACT.Exp).then_inc(ex_ok, 1)

                evacuate_x3(b0)
                split_w2(b0 + 2, 0, 1)
                split_x3t(b0)
                evacuate_x3(b0 + 1)
                split_w2(b0 + 2, 1, 2)
                split_w2(b0 + 2, 2, 4)
                exp_gap(b0)
                for j in range(HB):
                    b = b0 + j
                    if j < 2:
                        split_x3t(b + 1)
                    if j == 0:
                        split_w2(b0 + 3, 0, 2)
                    if h == 0 and j == 1:
                        split_x(1, 0)
                        split_x(1, 1)
                    act.wait_ge(hgt_mm, b + 1)
                    hi(hg_hi[:, b % 2], bank[HGT_BANK][:, 0:P], "hgt")
                    if j == 2:
                        exp_gap(b + 1)
                    act.wait_ge(hg_ok, b + 1)
                    if b >= 2:
                        act.wait_ge(out_done[b % 2], 16 * (b // 2))
                    nc.scalar.copy(res[:, b % 2, H:D], pair[b % 2][:, 1, 0:H]).then_inc(base_ok, 1)
                    if j == 0:
                        split_w2(b0 + 3, 2, 4)
                    if h == 0 and j == 1:
                        split_x(1, 2)
                    if j < 2:
                        evacuate_x3(b + 2)
                    if h == 0 and j == 1:
                        split_x(1, 3)
                    if j == 1:
                        split_x3t(b + 2)
                    act.wait_ge(low_mm, b + 1)
                    nc.scalar.copy(res[:, b % 2, 0:H], pair[b % 2][:, 0, 0:H]).then_inc(low_ok, 1)
                    if j < 2:
                        exp_gap(b + 1)
                    if h == 0 and j == 2:
                        split_w2(HB, 0, 2)
                    if h == 0 and j == 3:
                        split_w2(HB, 2, 4)
                        split_w2(HB + 1, 0, 2)
                        split_w2(HB + 1, 2, 4)

        @block.vector
        def _(dve):
            links = [0]

            def link(ins):
                links[0] += 1
                ins.then_inc(chain, 1)
                dve.wait_ge(chain, links[0])

            count = {}

            def lo(dst, src, hi_part, name, parts=1):
                count[name] = count.get(name, 0) + parts
                dve.wait_ge(S[name + "_hi"], count[name])
                return dve.tensor_tensor(dst, src, hi_part.bitcast(F32), ALU.subtract).then_inc(S[name + "_lo"], parts)

            def split_x(h, k):
                lo(x_lo[:, k], slot(f"x{h}")[:, k], x_hi[:, k], "x")

            def split_w1(k):
                lo(w1_lo[:, k], slot("w1")[:, k], w1_hi[:, k], "w1")

            def split_w2(b, k0, k1):
                lo(w2_lo[:, b % 2, k0:k1], slot(f"w2_{b}")[:, k0:k1], w2_hi[:, b % 2, k0:k1], "w2", k1 - k0)

            dve.memset(x3[:, 0, 0:D // 2], 0.0).then_inc(warm_ok, 1)
            dve.wait_ge(eye_ok, 1)
            for k in range(K):
                dve.wait_ge(w1_in[k], 16)
                d = slot("w1")[:, k, k * P:(k + 1) * P]
                dve.tensor_tensor(d, d, ident, ALU.add).then_inc(w1_eye, 1)
                split_w1(k)
                split_x(0, k)
            lo(a0_lo[:], a0t_bank.rearrange("p (k c) -> p k c", k=K), a0_hi[:], "a0")
            lo(a1_lo[:], a1t_bank.rearrange("p (k c) -> p k c", k=K), a1_hi[:], "a1")
            b0t = b0t_bank.rearrange("p (k c) -> p k c", k=K)
            dve.wait_ge(S["dnu_hi"], 2)
            lo(dn_lo[:, :, 0, 0:HR], b0t[:, :, 0:HR], dn_hi[:, :, 0, 0:HR], "dnu")
            lo(dn_lo[:, :, 1, HR:P], b0t[:, :, HR:P], dn_hi[:, :, 1, HR:P], "dnu")
            lo(b0_lo[:], g0[:, 0], b0_hi[:], "b0")
            dve.wait_ge(cst_in, 16)
            dve.wait_ge(g_mm, 1)
            dve.tensor_tensor(gm[:], g_bank[:, 0:P], cst[:, C_GMASK:C_GMASK + P], ALU.mult).then_inc(gm_ok, 1)
            lo(g_lo[:], gm[:], g_hi[:], "g")
            lo(w3_lo[:, :, D:D + AR], ar_in[:], w3_hi[:, :, D:D + AR], "ar")
            lo(b3_lo[:], b3_in[:], b3_hi[:], "b3")
            dve.wait_ge(bg_mm, 1)
            dve.wait_ge(a1_ok, 1)
            dve.tensor_tensor(a1[:], bg_bank.rearrange("p (k c) -> p k c", k=K), a1[:], ALU.add) \
               .then_inc(a1g_ok, 1)
            lo(dn_lo[:, :, 0, HR:P], a1[:, :, HR:P], dn_hi[:, :, 0, HR:P], "dnv")
            lo(dn_lo[:, :, 1, 0:HR], a1[:, :, 0:HR], dn_hi[:, :, 1, 0:HR], "dnv")
            ids3 = ids[:, I_LANG:I_LANG + B].rearrange("p (b e) -> p b e", e=1).to_broadcast([P, B, E])
            link(dve.tensor_tensor(onehot[:], ids3, iota[:, None, :].to_broadcast([P, B, E]), ALU.is_equal))
            link(dve.tensor_scalar(bias[:], onehot[:], LANG_BIAS, None, ALU.mult))
            split_w2(0, 0, 2)
            split_w2(0, 2, 4)

            for h in range(2):
                b0 = HB * h
                dve.wait_ge(uv_mm, h + 1)
                mask = cst[:, C_UVMASK:C_UVMASK + HB].rearrange("p (j t) -> p j t", t=1).to_broadcast([P, HB, P])
                dve.tensor_tensor(uv[:].rearrange("p (j t) -> p j t", j=HB),
                                  uv_bank.rearrange("p (j t) -> p j t", j=HB), mask, ALU.mult) \
                   .then_inc(uv_ok, 1)
                if h == 0:
                    lo(up_lo[:, 0], g1[:, 0], up_hi[:, 0], "up")
                lo(uv_lo[:], uv[:], uv_hi[:], "uv")
                if h == 0:
                    split_w2(1, 0, 1)
                for o in range(K):
                    lo(x2_lo[:, o], bank[L1_BANK + o][:], x2_hi[:, o], "x2")
                if h == 0:
                    split_w2(1, 1, 2)
                    split_w2(1, 2, 4)

                def split_x3t(b):
                    lo(x3_lo[:, b % 2].rearrange("p k t -> p (k t)"), bank[X3T_BANK][:],
                       x3_hi[:, b % 2].rearrange("p k t -> p (k t)"), "x3t")

                def route(b):
                    q = b % 2
                    dve.wait_ge(ar_mm, b + 1)
                    link(dve.tensor_tensor(logits[:, q], pair[q][:, 1, H + E * R:H + AR], bias[:, b], ALU.add))
                    link(dve.max(top[:, q], logits[:, q]))
                    dve.tensor_tensor(gap[:, q], top[:, q, 1:2], top[:, q, 0:1], ALU.subtract).then_inc(gap_ok, 1)
                    link(dve.max_index(topi[:, q], top[:, q], logits[:, q]))
                    at = topi[:, q, 0:2].rearrange("p (s e) -> p s e", e=1).to_broadcast([P, 2, E])
                    dve.tensor_tensor(hot[:, q], at, iota[:, None, :].to_broadcast([P, 2, E]), ALU.is_equal) \
                       .then_inc(chain, 1)
                    links[0] += 1

                def gates(b):
                    q = b % 2
                    dve.wait_ge(ex_ok, b + 1)
                    dve.wait_ge(chain, links[0])
                    dve.tensor_scalar(rden[:, q, 0:1], ex[:, q], 0.5, 0.5, ALU.mult, ALU.add).then_inc(chain, 1)
                    dve.scalar_tensor_tensor(out=gate[:, q], in0=hot[:, q, 1], scalar=ex[:, q, 0:1], in1=hot[:, q, 0],
                                             op0=ALU.mult, op1=ALU.add).then_inc(chain, 1)
                    links[0] += 2
                    dve.wait_ge(chain, links[0])
                    link(dve.reciprocal(rden[:, q, 1:2], rden[:, q, 0:1]))
                    g = gate[:, q].rearrange("p (e r) -> p e r", r=1).to_broadcast([P, E, R])
                    dve.scalar_tensor_tensor(out=hg[:, q].rearrange("p (e r) -> p e r", e=E),
                                             in0=pair[q][:, 1, H:H + E * R].rearrange("p (e r) -> p e r", e=E),
                                             scalar=rden[:, q, 1:2], in1=g, op0=ALU.mult, op1=ALU.mult) \
                       .then_inc(hg_ok, 1)

                split_w2(b0 + 2, 0, 1)
                split_x3t(b0)
                split_w2(b0 + 2, 1, 2)
                split_w2(b0 + 2, 2, 3)
                route(b0)
                gates(b0)
                split_w2(b0 + 2, 3, 4)
                for j in range(HB):
                    b = b0 + j
                    if j < 2:
                        split_x3t(b + 1)
                    if h == 0 and j == 1:
                        split_x(1, 0)
                        split_x(1, 1)
                    if j == 2:
                        route(b + 1)
                    lo(hg_lo[:, b % 2], bank[HGT_BANK][:, 0:P], hg_hi[:, b % 2], "hgt")
                    if j == 0:
                        split_w2(b0 + 3, 0, 2)
                        split_w2(b0 + 3, 2, 4)
                    if h == 0 and j == 1:
                        split_x(1, 2)
                        split_x(1, 3)
                    if j == 2:
                        gates(b + 1)
                    dve.wait_ge(high_mm, b + 1)
                    dve.wait_ge(base_ok, b + 1)
                    dve.tensor_tensor(res[:, b % 2, H:D], up_high, res[:, b % 2, H:D], ALU.add).then_inc(high_ok, 1)
                    if j == 1:
                        split_x3t(b + 2)
                    if j < 2:
                        route(b + 1)
                        gates(b + 1)
                    if h == 0 and j == 0:
                        lo(up_lo[:, 1], g1[:, 1], up_hi[:, 1], "up")
                    if h == 0 and j == 2:
                        split_w2(HB, 0, 2)
                    if h == 0 and j == 3:
                        split_w2(HB, 2, 4)
                        split_w2(HB + 1, 0, 2)
                        split_w2(HB + 1, 2, 4)

        @block.tensor
        def _(pe):
            def product(out, lhs, rhs, first=True, last=True):
                nc.tensor.matmul(out, lhs[0], rhs[0], start=first, stop=False)
                nc.tensor.matmul(out, lhs[1], rhs[0], start=False, stop=False)
                return nc.tensor.matmul(out, lhs[0], rhs[1], start=False, stop=last)

            def layer1_first():
                for (w, x), ready in (((w1_hi, x_hi), ("w1_hi", "x_hi")), ((w1_lo, x_hi), ("w1_lo",)),
                                      ((w1_hi, x_lo), ("x_lo",))):
                    for n in ready:
                        pe.wait_ge(S[n], 1)
                    for o in range(K):
                        nc.tensor.matmul(bank[L1_BANK + o][:], w[:, 0, o * P:(o + 1) * P], x[:, 0],
                                         start=(ready[0] == "w1_hi"), stop=False)

            def layer1(h, k, chunks=range(K)):
                pe.wait_ge(S["x_lo"], K * h + k + 1)
                pe.wait_ge(S["w1_lo"], k + 1)
                for o in chunks:
                    if h and k == 0 and o == HGT_BANK:
                        pe.wait_ge(high_ok, HB)
                    c = slice(o * P, (o + 1) * P)
                    last = product(bank[L1_BANK + o][:], (w1_hi[:, k, c], w1_lo[:, k, c]), (x_hi[:, k], x_lo[:, k]),
                                   first=(k == 0), last=False)
                return last

            def down(h):
                pe.wait_ge(S["x_lo"], K * (h + 1))
                if h:
                    pe.wait_ge(high_ok, HB - 1)
                pe.wait_ge(S["dnu_lo"], 2)
                pe.wait_ge(S["dnv_lo"], 2)
                for k in range(K):
                    last = product(uv_bank, (dn_hi[:, k, h], dn_lo[:, k, h]), (x_hi[:, k], x_lo[:, k]),
                                   first=(k == 0), last=(k == K - 1))
                last.then_inc(uv_mm, 1)

            def up(h):
                pe.wait_ge(S["uv_lo"], h + 1)
                pe.wait_ge(S["up_lo"], h + 1)
                for o in range(K):
                    c = slice(o * P, (o + 1) * P)
                    product(bank[L1_BANK + o][:], (up_hi[:, h, c], up_lo[:, h, c]), (uv_hi[:], uv_lo[:]),
                            first=False).then_inc(x2_mm, 1)

            def transposes(dst, src):
                for k in range(K):
                    last = nc.tensor.transpose(dst[:, k * P:(k + 1) * P], src[:, k * P:(k + 1) * P], ident)
                return last

            def layer2(b, chunks=range(K)):
                j = b % HB
                t = slice(j * P, (j + 1) * P)
                for k in chunks:
                    pe.wait_ge(S["x2_lo"], K * (b // HB) + (k + 1 if j == 0 else K))
                    pe.wait_ge(S["w2_lo"], K * b + k + 1)
                    if k == 0 and j >= 2:
                        pe.wait_ge(x3_ok, b - 1)
                    last = product(bank[X3_BANK + b % 2][:], (x2_hi[:, k, t], x2_lo[:, k, t]),
                                   (w2_hi[:, b % 2, k], w2_lo[:, b % 2, k]), first=(k == 0), last=(k == K - 1))
                if K - 1 in chunks:
                    last.then_inc(x3_mm, 1)

            def transpose_x3(b):
                pe.wait_ge(x3_ok, b + 1)
                if b % HB:
                    pe.wait_ge(S["x3t_lo"], b)
                transposes(bank[X3T_BANK], x3[:, b % 2]).then_inc(x3t_mm, 1)

            def down3(b, chunks):
                q = b % 2
                if 0 in chunks:
                    pe.wait_ge(S["x3t_lo"], b + 1)
                    pe.wait_ge(S["ar_lo"], 1)
                    pe.wait_ge(S["w3_lo"], 2)
                    if b >= 2:
                        pe.wait_ge(high_ok, b - 1)
                for k in chunks:
                    last = product(pair[q][:, 1, 0:H + AR], (x3_hi[:, q, k], x3_lo[:, q, k]),
                                   (w3_hi[:, k, H:D + AR], w3_lo[:, k, H:D + AR]), first=(k == 0), last=(k == K - 1))
                if K - 1 in chunks:
                    last.then_inc(ar_mm, 1)

            def layer3(b, chunks):
                q = b % 2
                if 0 in chunks and b >= 2:
                    pe.wait_ge(low_ok, b - 1)
                for k in chunks:
                    product(pair[q][:, 0, 0:H], (x3_hi[:, q, k], x3_lo[:, q, k]), (w3_hi[:, k, 0:H], w3_lo[:, k, 0:H]),
                            first=(k == 0), last=False)

            def transpose_hg(b):
                pe.wait_ge(hg_ok, b + 1)
                if b:
                    pe.wait_ge(S["hgt_lo"], b)
                    pe.wait_ge(high_ok, b)
                nc.tensor.transpose(bank[HGT_BANK][:, 0:P], hg[:, b % 2], ident).then_inc(hgt_mm, 1)

            def up3(b):
                q = b % 2
                pe.wait_ge(S["hgt_lo"], b + 1)
                pe.wait_ge(S["b3_lo"], 1)
                hg_parts = (hg_hi[:, q], hg_lo[:, q])
                product(up_high, hg_parts, (b3_hi[:, H:D], b3_lo[:, H:D])).then_inc(high_mm, 1)
                product(pair[q][:, 0, 0:H], hg_parts, (b3_hi[:, 0:H], b3_lo[:, 0:H]), first=False).then_inc(low_mm, 1)

            pe.wait_ge(warm_ok, 1)
            for _ in range(WARM_UP):
                nc.tensor.matmul(g_bank, warm[:, 0:P], warm, start=True, stop=True)
            layer1_first()
            layer1(0, 1, range(2))
            pe.wait_ge(eye_ok, 1)
            pe.wait_ge(g0_in, 16)
            transposes(a0t_bank, g0[:, 1]).then_inc(a0t_mm, 1)
            transposes(b0t_bank, g0[:, 0]).then_inc(b0t_mm, 1)
            layer1(0, 1, [2])
            pe.wait_ge(g1_in, 16)
            transposes(a1t_bank, g1[:, 0]).then_inc(a1t_mm, 1)
            layer1(0, 1, [3])
            layer1(0, 2, range(2))
            pe.wait_ge(S["a0_lo"], 1)
            pe.wait_ge(S["a1_lo"], 1)
            for k in range(K):
                last = product(g_bank[:, 0:P], (a0_hi[:, k], a0_lo[:, k]), (a1_hi[:, k], a1_lo[:, k]),
                               first=(k == 0), last=(k == K - 1))
            last.then_inc(g_mm, 1)
            layer1(0, 2, range(2, K))
            pe.wait_ge(S["g_lo"], 1)
            pe.wait_ge(S["b0_lo"], 1)
            pe.wait_ge(S["dnu_lo"], 2)
            for k in range(K):
                c = slice(k * P, (k + 1) * P)
                last = product(bg_bank[:, c], (b0_hi[:, c], b0_lo[:, c]), (g_hi[:], g_lo[:]))
            last.then_inc(bg_mm, 1)
            pe.wait_ge(S["w1_lo"], K)
            for k in range(K):
                last = product(aw_bank, (a0_hi[:, k], a0_lo[:, k]), (w1_hi[:, k], w1_lo[:, k]),
                               first=(k == 0), last=(k == K - 1))
            last.then_inc(aw_mm, 1)
            down(0)
            layer1(0, 3).then_inc(l1x_mm, 1)
            up(0)

            for h in range(2):
                b0 = HB * h
                layer2(b0)
                layer2(b0 + 1, range(2))
                transpose_x3(b0)
                layer2(b0 + 1, range(2, K))
                layer2(b0 + 2, [0])
                down3(b0, range(K))
                transpose_x3(b0 + 1)
                layer3(b0, range(K))
                layer2(b0 + 2, [1])
                transpose_hg(b0)
                layer2(b0 + 2, range(2, K))
                down3(b0 + 1, [0])
                up3(b0)
                down3(b0 + 1, range(1, K))
                transpose_x3(b0 + 2)
                layer2(b0 + 3, range(3))
                transpose_hg(b0 + 1)
                layer2(b0 + 3, [3])
                layer3(b0 + 1, range(K))
                transpose_x3(b0 + 3)
                up3(b0 + 1)
                down3(b0 + 2, range(K))
                down3(b0 + 3, range(K))
                layer3(b0 + 2, [0])
                transpose_hg(b0 + 2)
                layer3(b0 + 2, range(1, K))
                up3(b0 + 2)
                layer3(b0 + 3, [0])
                transpose_hg(b0 + 3)
                layer3(b0 + 3, range(1, K))
                if h == 0:
                    down(1)
                up3(b0 + 3)
                if h == 0:
                    for k in range(K):
                        layer1(1, k)
                    up(1)


_OUT = (B, P, D)


def kernel(**inputs):
    import numpy as np
    import concourse.bacc as bacc
    from concourse.bass_utils import run_bass_kernel_spmd

    a = {n: np.asarray(v) for n, v in inputs.items()}
    part = np.arange(P)
    consts = np.zeros((P, C_COLS), np.float32)
    consts[:, C_GMASK:C_GMASK + P] = part[:, None] // R == (part[None, :] // R + HB) % B
    consts[:, C_UVMASK:C_UVMASK + HB] = (part[:, None] % HR) // R == np.arange(HB)[None, :]
    consts[:, C_IOTA:C_IOTA + E] = np.arange(E)
    id0, id1, id3 = (a[n].reshape(B) for n in ("itok_B_3_7", "itok_B_0_15", "itok_B_0_7"))
    spread = lambda v: np.broadcast_to(v[None, :], (P, B))
    ints = np.concatenate([np.repeat(id0, R)[:, None], np.repeat(np.concatenate([id1[HB:], id1[:HB]]), R)[:, None],
                           (part % R).astype(id0.dtype)[:, None], spread(id3), spread(id0)], 1)
    t = np.transpose
    arrays = {
        "consts": consts,
        "ints": ints,
        "xT": t(a["x"].reshape(2, T, K, P), (0, 2, 3, 1)),
        "w1": a["L1_cond_W"].reshape(K, P, D),
        "gather0": np.concatenate([a["L0_cond_B"], t(a["L0_cond_A"], (0, 2, 1))], 2).reshape(-1, 2 * D),
        "gather1": np.concatenate([t(a["L1_cond_lora_A"], (0, 2, 1)), a["L1_cond_lora_B"]], 2).reshape(-1, 2 * D),
        "w2T": t(a["L2_cond_weight"].reshape(E, D, K, P), (0, 3, 2, 1)),
        "w3T": t(a["L3_cond_W"].reshape(D, K, P), (2, 1, 0)),
        "ar": t(np.concatenate([a["L3_cond_A"].reshape(E * R, D), a["L3_cond_Wr"]], 0).reshape(AR, K, P), (2, 1, 0)),
        "b3": t(a["L3_cond_B"], (0, 2, 1)).reshape(E * R, D),
    }
    arrays = {n: np.ascontiguousarray(v) for n, v in arrays.items()}
    nc = bacc.Bacc("TRN2", target_bir_lowering=False, num_devices=1)
    args = [nc.dram_tensor(n, v.shape, mybir.dt.from_np(v.dtype), kind="ExternalInput").ap() for n, v in arrays.items()]
    args.append(nc.dram_tensor("out", _OUT, F32, kind="ExternalOutput").ap())
    cond_resid_kernel(nc, *args)
    r = run_bass_kernel_spmd(nc, [arrays], core_ids=[0])
    return r.results[0]["out"]
```
